# Optimizing a Trainium2 kernel written in Bass

```python
import numpy as np
import jax
import jax.numpy as jnp

def _softmax(x, axis=-1):
    return jax.nn.softmax(x, axis=axis)

def _gelu(x):
    return jax.nn.gelu(x, approximate=True)

def _silu(x):
    return jax.nn.silu(x)

def _sigmoid(x):
    return jax.nn.sigmoid(x)

def _layernorm(x, axis=-1, eps=1e-05):
    m = jnp.mean(x, axis=axis, keepdims=True)
    v = jnp.var(x, axis=axis, keepdims=True)
    return (x - m) / jnp.sqrt(v + eps)

def _scatter_add(tgt, idx, src, axis=0):
    return tgt.at[idx].add(src)

def _segment_sum(src, seg, n):
    return jax.ops.segment_sum(src, seg, n)
kernel_name = 'mk_adj_resnorm_d1_adj_r2_10415c'

def setup_inputs(seed: int=0):
    np.random.seed(seed)
    _w = jnp.asarray

    def _rec_inputs():
        import jax
        import jax.numpy as jnp
        _gk = jax.random.key(seed)
        x = -0.0002928 + 1 * jax.random.normal(jax.random.fold_in(_gk, 1), (32, 256, 256), jnp.float32)
        _a = jax.random.bernoulli(jax.random.fold_in(_gk, 2), 0.03125, (32, 256, 256))
        _a = jnp.logical_or(_a, jnp.swapaxes(_a, -1, -2))
        _a = jnp.logical_or(_a, jnp.eye(256, dtype=bool))
        adj = _a.astype(jnp.int32)
        return (x, adj)
    x, adj = _rec_inputs()

    def _L0_gnn_setup():
        import jax, jax.numpy as jnp
        import numpy as np
        L = 3
        D = 256
        B, N = (8, 512)
        EPS = 1e-05

        def layernorm(x, gamma, beta):
            mu = jnp.mean(x, axis=-1, keepdims=True)
            var = jnp.var(x, axis=-1, keepdims=True)
            return (x - mu) * jax.lax.rsqrt(var + EPS) * gamma + beta
        key = jax.random.key(seed)
        ks = jax.random.split(key, 12)
        s = 1.0 / np.sqrt(D)
        node_features = jax.random.normal(ks[0], (B, N, D), dtype=jnp.float32)
        adjacency_matrix = jax.random.randint(ks[1], (B, N, N), 0, 2, dtype=jnp.int32)
        return {'node_features': node_features, 'adjacency_matrix': adjacency_matrix, 'attn_w': jax.random.normal(ks[2], (L, 2 * D), dtype=jnp.float32) * (1.0 / np.sqrt(2 * D)), 'attn_b': jax.random.normal(ks[3], (L,), dtype=jnp.float32) * 0.01, 'W1': jax.random.normal(ks[4], (L, D, 4 * D), dtype=jnp.float32) * s, 'b1': jnp.zeros((L, 4 * D), dtype=jnp.float32), 'W2': jax.random.normal(ks[5], (L, 4 * D, D), dtype=jnp.float32) * (1.0 / np.sqrt(4 * D)), 'b2': jnp.zeros((L, D), dtype=jnp.float32), 'g1': jnp.ones((L, D), dtype=jnp.float32), 'beta1': jnp.zeros((L, D), dtype=jnp.float32), 'g2': jnp.ones((L, D), dtype=jnp.float32), 'beta2': jnp.zeros((L, D), dtype=jnp.float32)}
    _L0_gnn_all = _L0_gnn_setup()
    _L0_gnn_in = {k: v for k, v in _L0_gnn_all.items() if k in ('attn_w', 'attn_b', 'W1', 'b1', 'W2', 'b2', 'g1', 'beta1', 'g2', 'beta2')}
    del _L0_gnn_all
    return {'x': x, 'adj': adj, 'L0_gnn_attn_w': _L0_gnn_in['attn_w'], 'L0_gnn_attn_b': _L0_gnn_in['attn_b'], 'L0_gnn_W1': _L0_gnn_in['W1'], 'L0_gnn_b1': _L0_gnn_in['b1'], 'L0_gnn_W2': _L0_gnn_in['W2'], 'L0_gnn_b2': _L0_gnn_in['b2'], 'L0_gnn_g1': _L0_gnn_in['g1'], 'L0_gnn_beta1': _L0_gnn_in['beta1'], 'L0_gnn_g2': _L0_gnn_in['g2'], 'L0_gnn_beta2': _L0_gnn_in['beta2']}

def reference(x, adj, L0_gnn_attn_w, L0_gnn_attn_b, L0_gnn_W1, L0_gnn_b1, L0_gnn_W2, L0_gnn_b2, L0_gnn_g1, L0_gnn_beta1, L0_gnn_g2, L0_gnn_beta2):
    import jax
    import jax.numpy as jnp

    def _L0_gnn_ref(node_features, adjacency_matrix, attn_w, attn_b, W1, b1, W2, b2, g1, beta1, g2, beta2):
        import jax, jax.numpy as jnp
        import numpy as np
        L = 3
        D = 256
        B, N = (8, 512)
        EPS = 1e-05

        def layernorm(x, gamma, beta):
            mu = jnp.mean(x, axis=-1, keepdims=True)
            var = jnp.var(x, axis=-1, keepdims=True)
            return (x - mu) * jax.lax.rsqrt(var + EPS) * gamma + beta
        n = adjacency_matrix.shape[-1]
        mask = adjacency_matrix.astype(jnp.float32) + jnp.eye(n, dtype=jnp.float32) > 0
        x = node_features
        d = x.shape[-1]
        for l in range(attn_w.shape[0]):
            si = x @ attn_w[l, :d]
            sj = x @ attn_w[l, d:]
            scores = si[:, :, None] + sj[:, None, :] + attn_b[l]
            scores = jnp.where(scores >= 0, scores, 0.2 * scores)
            scores = jnp.where(mask, scores, -jnp.inf)
            attn = jax.nn.softmax(scores, axis=-1)
            agg = jnp.einsum('bij,bjd->bid', attn, x)
            h = layernorm(x + agg, g1[l], beta1[l])
            ff = jax.nn.gelu(h @ W1[l] + b1[l], approximate=False) @ W2[l] + b2[l]
            x = layernorm(h + ff, g2[l], beta2[l])
        return x
    x = _layernorm(x + _L0_gnn_ref(x, adj, L0_gnn_attn_w, L0_gnn_attn_b, L0_gnn_W1, L0_gnn_b1, L0_gnn_W2, L0_gnn_b2, L0_gnn_g1, L0_gnn_beta1, L0_gnn_g2, L0_gnn_beta2), axis=-1)
    return x

_drawn_inputs = setup_inputs


def setup_inputs(seed=0):
    import zlib

    import numpy as np

    out = dict(_drawn_inputs(seed))
    spreads = {'L0_gnn_b1': (0.0, 0.1),
     'L0_gnn_b2': (0.0, 0.1),
     'L0_gnn_g1': (1.0, 0.2),
     'L0_gnn_beta1': (0.0, 0.1),
     'L0_gnn_g2': (1.0, 0.2),
     'L0_gnn_beta2': (0.0, 0.1)}
    factors = {'L0_gnn_attn_b': 64.0}
    for name, (base, spread) in spreads.items():
        noise = np.random.default_rng([zlib.crc32(name.encode()), seed]).standard_normal(out[name].shape)
        drawn = base * np.exp(spread * noise) if base else spread * noise
        out[name] = jnp.asarray(drawn.astype(out[name].dtype))
    for name, factor in factors.items():
        out[name] = (out[name] * factor).astype(out[name].dtype)
    return out
```

```python
from contextlib import ExitStack, nullcontext

import concourse.bass as bass
from concourse import mybir

F32 = mybir.dt.float32
BF16 = mybir.dt.bfloat16
F16 = mybir.dt.float16
I32 = mybir.dt.int32
U8 = mybir.dt.uint8
ALU = mybir.AluOpType
ACT = mybir.ActivationFunctionType

P = 128
EPS = 1e-5
SLOPE = 0.2
MASKED = -3.0e38
LEAST = -3.4e38


class Unit:

    def __init__(self, pair, c):
        self.pair, self.c = pair, c
        self.par = c % 2
        self.half = pair + c // 2
        self.n = 2 * pair + c

    def plus(self, k):
        return Unit(self.pair, self.c + k)


def not_first(w):
    return not (isinstance(w.n, int) and w.n == 0)


def runs(keys, cuts):
    a = 0
    for b in range(1, len(keys) + 1):
        if b == len(keys) or keys[b] != keys[a] or b in cuts:
            yield a, b
            a = b


def over_pairs(eng, a, b):
    return eng.Fori(a, b) if b - a > 1 else nullcontext(a)


def gnn_kernel(nc, x, adj, attn_w, attn_b, W1, b1, W2, b2, g1, beta1, g2, beta2, out):
    B, N, D = x.shape
    L, _, F = W1.shape
    R = N // P
    G = 2
    T = G * R
    TOK = T * P
    KD = D // P
    FC = F // P
    PL = B // G
    U = L * PL
    PAIRS = U // 2
    TD = T * D
    NB1 = 3

    def layer(u):
        return u // PL if 0 <= u < U else None

    x_d = x.rearrange("(u g) (r q) d -> u q g r d", g=G, q=P)
    out_d = out.rearrange("(u g) (r q) d -> u q g r d", g=G, q=P)
    adj_d = adj.rearrange("(u g) (r q) j -> u q g r j", g=G, q=P)
    MASK_BYTES = P * T * N * 2
    mask_store = nc.dram_tensor("mask_store", [PL * MASK_BYTES], U8, kind="Internal").ap()

    with ExitStack() as ctx:
        def sb(name, shape, dt):
            return ctx.enter_context(nc.sbuf_tensor(name, shape, dt))

        def psum(name, shape, dt):
            return ctx.enter_context(nc.psum_tensor(name, shape, dt))

        def sem(name):
            return ctx.enter_context(nc.semaphore(name))

        x_store = sb("x_store", [P, PL * TD], F32)
        w_stage = [x_store[:, l * KD * F:(l + 1) * KD * F] for l in range(2 * L)]
        w1_stage = [w_stage[2 * l].rearrange("p (k f) -> p k f", k=KD) for l in range(L)]
        w2_stage = [w_stage[2 * l + 1].rearrange("p (c d) -> p c d", c=FC) for l in range(L)]
        w1_hi = sb("w1_hi", [P, L, KD, F], BF16)
        w1_lo = sb("w1_lo", [P, L, KD, F], BF16)
        w2_hi = sb("w2_hi", [P, L, FC, D], BF16)
        w2_lo = sb("w2_lo", [P, L, FC, D], BF16)
        g1_col = sb("g1_col", [P, L, KD], F32)
        beta1_col = sb("beta1_col", [P, L, KD], F32)
        b1_col = sb("b1_col", [P, L, FC], F32)
        g1_row = sb("g1_row", [P, L, D], F32)
        shift1_row = sb("shift1_row", [P, L, D], F32)
        g2_row = sb("g2_row", [P, L, D], F32)
        beta2_row = sb("beta2_row", [P, L, D], F32)
        attn_row = sb("attn_row", [P, L, 2 * D], F32)
        attn_b_row = sb("attn_b_row", [P, L], F32)
        ident = sb("ident", [P, P], F32)
        neg_eye = sb("neg_eye", [P, R, N], F32)
        eps_c = sb("eps_c", [P, T], F32)
        mhalf_c = sb("mhalf_c", [P, T], F32)

        x_in = [sb(f"x_in{i}", [P, T, D], F32) for i in range(2)]
        stage = [sb(f"stage{i}", [P, T, D], F32) for i in range(2)]
        adj_in = [s[:].bitcast(I32) for s in stage]
        x0_in, fin = stage
        mask = [sb(f"mask{i}", [P, T, N], BF16) for i in range(2)]
        junk = [sb(f"junk{i}", [P, D], F32) for i in range(2)]
        ty = sb("ty", [P, T, D], F32)
        e1 = sb("e1", [P, T, N], F32)
        e2 = sb("e2", [P, T, N], F32)
        pt_hi = sb("pt_hi", [P, G, R, N], F16)
        pt_lo = sb("pt_lo", [P, G, R, N], F16)
        x_hi = sb("x_hi", [P, T, D], BF16)
        x_lo = sb("x_lo", [P, T, D], BF16)
        nrm = [sb(f"nrm{i}", [P, T, D], F32) for i in range(2)]
        nt_hi = [sb(f"nt_hi{i}", [P, KD, TOK], F16) for i in range(2)]
        nt_lo = [sb(f"nt_lo{i}", [P, KD, TOK], F16) for i in range(2)]
        g_f = [sb(f"g_f{i}", [P, TOK], F32) for i in range(2)]
        g_hi = [sb(f"g_hi{i}", [P, TOK], BF16) for i in range(3)]
        g_lo = [sb(f"g_lo{i}", [P, TOK], BF16) for i in range(3)]
        zb = sb("zb", [P, T, D], F32)

        b2_row = zb[:, 0:L, :]

        dots = sb("dots", [P, 2, T], F32)
        smax = sb("smax", [P, T], F32)
        cb = sb("cb", [P, T], F32)
        zm = sb("zm", [P, T], F32)
        rmax = sb("rmax", [P, T], F32)
        bias1 = sb("bias1", [P, T], F32)
        bias2 = sb("bias2", [P, T], F32)
        den = sb("den", [P, T], F32)
        rden = sb("rden", [P, T], F32)
        bs = [sb(f"bs{i}", [P, T, 6], F32) for i in range(3)]
        mv = [sb(f"mv{i}", [P, T, 2], F32) for i in range(3)]
        rs = [sb(f"rs{i}", [P, T], F32) for i in range(3)]
        ve = [sb(f"ve{i}", [P, T], F32) for i in range(3)]
        marker = sb("marker", [P, 1], F32)
        nmr = sb("nmr", [P, T], F32)

        s_bank = psum("s_bank", [P, G, N], F32)
        xb = psum("xb", [P, 2 * 512], F32)
        f1_bank = [psum(f"f1_bank{i}", [P, TOK], F32) for i in range(NB1)]
        f2_bank = psum("f2_bank", [P, T, D], F32)
        xb_pt = xb[:].rearrange("p (g c i) -> p g c i", g=G, c=R)
        xb_agg = xb[:].rearrange("p (t d) -> p t d", t=T)
        xb_nt = xb[:].rearrange("p (k n) -> p k n", k=KD)

        s_x = [sem(f"s_x{i}") for i in range(2)]
        s_adj = [sem(f"s_adj{i}") for i in range(2)]
        s_mask = [sem(f"s_mask{i}") for i in range(2)]
        s_mstore = [sem(f"s_mstore{i}") for i in range(2)]
        s_xstore = [sem(f"s_xstore{i}") for i in range(2)]
        s_x0 = sem("s_x0in")
        s_out = sem("s_out")
        s_attn_p = sem("s_attn_p")
        s_col = sem("s_col")
        s_row = sem("s_row")
        s_w = [sem(f"s_w{i}") for i in range(2 * L)]
        s_const = sem("s_const")
        s_ident = sem("s_ident")
        s_whi = sem("s_whi")
        s_wlo = sem("s_wlo")
        s_b1ps = sem("s_b1ps")
        s_b1 = sem("s_b1")
        s_shift = sem("s_shift")
        s_dots = sem("s_dots")
        s_conv1 = sem("s_conv1")
        s_conv = sem("s_conv")
        s_sj = sem("s_sj")
        s_smax = sem("s_smax")
        s_bstep = sem("s_bstep")
        s_bias = sem("s_bias")
        s_exp = sem("s_exp")
        s_p = sem("s_p")
        s_rden = sem("s_rden")
        s_pt = sem("s_pt")
        s_pthi = sem("s_pthi")
        s_ptlo = sem("s_ptlo")
        s_xhi = sem("s_xhi")
        s_xlo = sem("s_xlo")
        s_agg = sem("s_agg")
        s_y = sem("s_y")
        s_bn = [sem(f"s_bn{i}") for i in range(3)]
        s_mv = [sem(f"s_mv{i}") for i in range(3)]
        s_ve = [sem(f"s_ve{i}") for i in range(3)]
        s_rs = [sem(f"s_rs{i}") for i in range(3)]
        s_n1 = sem("s_n1")
        s_nt = sem("s_nt")
        s_nthi = sem("s_nthi")
        s_ntlo = sem("s_ntlo")
        s_f1 = sem("s_f1")
        s_gelu = sem("s_gelu")
        s_ghi = sem("s_ghi")
        s_glo = sem("s_glo")
        s_f2 = sem("s_f2")
        s_hb1 = sem("s_hb1")
        s_hb = sem("s_hb")
        s_z = sem("s_z")
        s_n2 = sem("s_n2")
        s_xa1 = sem("s_xa1")
        s_xa = sem("s_xa")
        s_fin = sem("s_fin")
        s_nmr = sem("s_nmr")
        s_norm3 = sem("s_norm3")

        FIN0 = (L - 1) * PL
        CUTS = (1, FIN0 // 2 + 1, FIN0 // 2 + 2)

        def stored_mask(at):
            return mask_store[bass.ds(at, MASK_BYTES)].rearrange("(q b) -> q b", q=P)

        def mask_bytes(w):
            return mask[w.par][:].rearrange("q t d -> q (t d)").bitcast(U8)

        block = ctx.enter_context(nc.Block())

        @block.sync
        def _(sp):
            def load_x(w, l, p):
                if l == 0:
                    src = x_d[p]
                else:
                    sp.wait_ge(s_xstore[w.par], 16 * (w.half - PL // 2 + 1))
                    src = x_store[:, bass.ts(p, TD)].rearrange("q (t d) -> q t d", t=T)
                dst = x_in[w.par][:].rearrange("q (g r) d -> q g r d", g=G) if l == 0 else x_in[w.par][:]
                sp.dma_start(dst, src).then_inc(s_x[w.par], 16)

            def load_adj(w, p):
                dst = adj_in[w.par].rearrange("q (g r) d -> q g r d", g=G)
                sp.dma_start(dst, adj_d[p]).then_inc(s_adj[w.par], 16)

            def load_mask(w, l, at):
                if l == 1:
                    sp.wait_ge(s_mstore[w.par], 16 * (PL // 2))
                sp.wait_ge(s_smax, w.n - 1)
                sp.dma_start(mask_bytes(w), stored_mask(at)).then_inc(s_mask[w.par], 16)

            def row(dst, src, s):
                sp.dma_start(dst, src).then_inc(s, 16)

            u0 = Unit(0, 0)
            load_x(u0, 0, 0)
            row(attn_row[:], attn_w.partition_broadcast(P), s_attn_p)
            row(attn_b_row[:], attn_b.partition_broadcast(P), s_attn_p)
            load_adj(u0, 0)
            load_x(u0.plus(1), 0, 1)
            load_adj(u0.plus(1), 1)
            with nc.allow_non_contiguous_dma(reason="a few parameters, feature on the partition"):
                row(g1_col[:], g1.rearrange("l (k p) -> p l k", p=P), s_col)
                row(beta1_col[:], beta1.rearrange("l (k p) -> p l k", p=P), s_col)
                row(b1_col[:], b1.rearrange("l (c p) -> p l c", p=P), s_col)
            for l in range(L):
                sp.dma_start(w1_stage[l], W1[l].rearrange("(k p) f -> p k f", p=P)).then_inc(s_w[2 * l], 16)
                sp.dma_start(w2_stage[l], W2[l].rearrange("(c p) d -> p c d", p=P)).then_inc(s_w[2 * l + 1], 16)
                if l == 0:
                    row(g1_row[:], g1.partition_broadcast(P), s_row)
                    row(shift1_row[:], beta1.partition_broadcast(P), s_row)
                    row(b2_row, b2.partition_broadcast(P), s_row)
                    row(g2_row[:], g2.partition_broadcast(P), s_row)
                    row(beta2_row[:], beta2.partition_broadcast(P), s_row)
            for k in range(2):
                sp.wait_ge(s_conv, k + 1)
                load_adj(u0.plus(k + 2), k + 2)
            sp.wait_ge(s_y, T)
            load_x(u0.plus(2), 0, 2)
            sp.wait_ge(s_wlo, 2 * L)
            sp.wait_ge(s_whi, 2 * L)
            sp.wait_ge(s_b1ps, 1)

            def step_key(u):
                return (layer(u - 1), layer(u + 3), layer(u + 4), layer(u - 2))

            def step(u, key):
                l_prev, l_x, l_next, l_fin = key
                last = L - 1

                places = {}
                for k, l in ((-1, l_prev), (-2, l_fin), (3, l_x), (4, l_next)):
                    if l is not None:
                        v = u.n + k - PL * l
                        if k == 4 and l > 0:
                            v = v * MASK_BYTES
                        places[k, l] = v if isinstance(v, int) else sp.snap(v)

                def at(k, l):
                    return places[k, l]
                if l_prev == last:
                    v = u.plus(-1)
                    if not (isinstance(v.n, int) and v.n == FIN0):
                        sp.wait_ge(s_fin, v.n - FIN0)
                    sp.dma_start(x0_in[:].rearrange("q (g r) d -> q g r d", g=G), x_d[at(-1, last)])\
                      .then_inc(s_x0, 16)
                elif l_prev is not None:
                    v = u.plus(-1)
                    sp.wait_ge(s_xa, v.n + 1)
                    sp.dma_start(x_store[:, bass.ts(at(-1, l_prev), TD)].rearrange("q (t d) -> q t d", t=T),
                                 zb[:]).then_inc(s_xstore[v.par], 16)
                if l_fin == last:
                    v = u.plus(-2)
                    sp.wait_ge(s_norm3, v.n - FIN0 + 1)
                    sp.dma_start(out_d[at(-2, last)], fin[:].rearrange("q (g r) d -> q g r d", g=G))\
                      .then_inc(s_out, 16)
                if l_x is not None:
                    v = u.plus(3)
                    sp.wait_ge(s_y, T * (v.n - 1))
                    load_x(v, l_x, at(3, l_x))
                if l_next == 0:
                    v = u.plus(4)
                    sp.wait_ge(s_conv, v.n - 1)
                    load_adj(v, at(4, 0))
                elif l_next is not None:
                    load_mask(u.plus(4), l_next, at(4, l_next))

            keys = [(step_key(2 * j), step_key(2 * j + 1)) for j in range(PAIRS + 1)]
            for a, b in runs(keys, CUTS):
                with over_pairs(sp, a, b) as j:
                    for c in range(2):
                        step(Unit(j, c), keys[a][c])
            sp.wait_ge(s_out, 16 * PL)

        @block.tensor
        def _(pe):
            def scores(w):
                pe.wait_ge(s_dots, 2 * T * (w.n + 1))
                pe.wait_ge(s_smax, w.n)
                for t in range(T):
                    mm = pe.transpose(s_bank[:, t // R, (t % R) * P:(t % R + 1) * P],
                                      dots[:, 1, t:t + 1].to_broadcast([P, P]), ident[:])
                mm.then_inc(s_sj, 1)

            def p_transposes(w):
                pe.wait_ge(s_p, T * (w.n + 1))
                pe.wait_ge(s_ntlo, w.n)
                for t in range(T):
                    for c in range(R):
                        mm = pe.transpose(xb_pt[:, t // R, c, (t % R) * P:(t % R + 1) * P],
                                          e1[:, t, c * P:(c + 1) * P], ident[:])
                mm.then_inc(s_pt, 1)

            def aggregate(w):
                pe.wait_ge(s_ptlo, w.n + 1)
                pe.wait_ge(s_xlo, w.n + 1)
                for t in range(T):
                    g, r = t // R, t % R
                    parts = [(a, b, c) for c in range(R) for a, b in ((pt_hi, x_hi), (pt_hi, x_lo), (pt_lo, x_hi))]
                    for i, (a, b, c) in enumerate(parts):
                        mm = pe.matmul(xb_agg[:, t, :], a[:, g, c, r * P:(r + 1) * P], b[:, g * R + c, :],
                                       start=(i == 0), stop=(i == len(parts) - 1))
                    if r == R - 1:
                        mm.then_inc(s_agg, 1)

            def n_transposes(w):
                pe.wait_ge(s_n1, w.n + 1)
                for k in range(KD):
                    for t in range(T):
                        mm = pe.transpose(xb_nt[:, k, t * P:(t + 1) * P],
                                          nrm[w.par][:, t, k * P:(k + 1) * P], ident[:])
                mm.then_inc(s_nt, 1)

            def hidden(u, l, c):
                if c == 0:
                    pe.wait_ge(s_ntlo, u.n + 1)
                pe.wait_ge(s_gelu, FC * u.n + max(0, c - NB1 + 1))
                parts = [(a, b, k) for k in range(KD) for a, b in ((w1_hi, nt_hi), (w1_hi, nt_lo), (w1_lo, nt_hi))]
                for i, (a, b, k) in enumerate(parts):
                    mm = pe.matmul(f1_bank[c % NB1][:], a[:, l, k, c * P:(c + 1) * P], b[u.par][:, k, :],
                                   start=(i == 0), stop=(i == len(parts) - 1))
                mm.then_inc(s_f1, 1)

            def project(u, l, c):
                pe.wait_ge(s_glo, FC * u.n + c + 1)
                if c == 0:
                    pe.wait_ge(s_z, u.n)
                for t in range(T):
                    for i, (a, b) in enumerate(((g_hi, w2_hi), (g_hi, w2_lo), (g_lo, w2_hi))):
                        mm = pe.matmul(f2_bank[:, t, :], a[c % 3][:, t * P:(t + 1) * P], b[:, l, c, :],
                                       start=(c == 0 and i == 0 and t % 2 == 0), stop=(c == FC - 1 and i == 2),
                                       skip_group_check=True)
                mm.then_inc(s_f2, 1)

            pe.wait_ge(s_ident, 1)
            scores(Unit(0, 0))
            scores(Unit(0, 1))
            p_transposes(Unit(0, 0))
            aggregate(Unit(0, 0))
            pe.wait_ge(s_col, 48)
            for l in range(L):
                pe.wait_ge(s_w[2 * l], 16)
                for c in range(FC):
                    for k in range(KD):
                        mm = pe.matmul(f1_bank[0][:, l * FC + c:l * FC + c + 1], w1_stage[l][:, k, c * P:(c + 1) * P],
                                       beta1_col[:, l, k:k + 1], start=(k == 0), stop=(k == KD - 1))
            mm.then_inc(s_b1ps, 1)
            n_transposes(Unit(0, 0))
            pe.wait_ge(s_b1, 1)
            pe.wait_ge(s_wlo, 2 * L)
            pe.wait_ge(s_whi, 2 * L)

            def iteration(u, l, mid, front):
                hidden(u, l, 0)
                hidden(u, l, 1)
                hidden(u, l, 2)
                if mid:
                    p_transposes(u.plus(1))
                project(u, l, 0)
                hidden(u, l, 3)
                project(u, l, 1)
                if mid:
                    aggregate(u.plus(1))
                hidden(u, l, 4)
                project(u, l, 2)
                hidden(u, l, 5)
                if front:
                    scores(u.plus(2))
                project(u, l, 3)
                hidden(u, l, 6)
                if mid:
                    n_transposes(u.plus(1))
                project(u, l, 4)
                hidden(u, l, 7)
                for c in range(5, FC):
                    project(u, l, c)

            keys = [tuple((layer(2 * j + c), layer(2 * j + c + 1) is not None, layer(2 * j + c + 2) is not None)
                          for c in range(2)) for j in range(PAIRS)]
            for a, b in runs(keys, CUTS):
                with over_pairs(pe, a, b) as j:
                    for c in range(2):
                        iteration(Unit(j, c), *keys[a][c])

        @block.scalar
        def _(act):
            def exps(w):
                act.wait_ge(s_bias, w.n + 1)
                act.wait_ge(s_pt, w.n)
                for t in range(T):
                    act.activation(e1[:, t, :], ty[:, t, :], ACT.Exp, bias=bias1[:, t:t + 1]).then_inc(s_exp, 1)
                    act.activation(e2[:, t, :], ty[:, t, :], ACT.Exp, bias=bias2[:, t:t + 1],
                                   scale=SLOPE).then_inc(s_exp, 1)

            def p_high(w):
                act.wait_ge(s_pt, w.n + 1)
                act.wait_ge(s_agg, G * w.n)
                act.activation(pt_hi[:].rearrange("p g c i -> p (g c i)"), xb[:], ACT.Identity).then_inc(s_pthi, 1)

            def x_high(w):
                act.wait_ge(s_x[w.par], 16 * (w.half + 1))
                act.wait_ge(s_agg, G * w.n)
                act.activation(x_hi[:], x_in[w.par][:], ACT.Identity).then_inc(s_xhi, 1)

            def n_high(w):
                act.wait_ge(s_nt, w.n + 1)
                act.activation(nt_hi[w.par][:].rearrange("p k n -> p (k n)"), xb[:], ACT.Identity)\
                   .then_inc(s_nthi, 1)

            def gelu(u, l, c):
                act.wait_ge(s_f1, FC * u.n + c + 1)
                act.wait_ge(s_glo, FC * u.n + max(0, c - 1))
                act.activation(g_f[c % 2][:], f1_bank[c % NB1][:], ACT.Gelu, bias=b1_col[:, l, c:c + 1])\
                   .then_inc(s_gelu, 1)

            def g_high(u, c):
                act.wait_ge(s_gelu, FC * u.n + c + 1)
                act.wait_ge(s_f2, FC * u.n + max(0, c - 2))
                act.activation(g_hi[c % 3][:], g_f[c % 2][:], ACT.Identity).then_inc(s_ghi, 1)

            def store_mask(w):
                act.wait_ge(s_conv, w.n + 1)
                act.dma_start(stored_mask(w.n * MASK_BYTES), mask_bytes(w)).then_inc(s_mstore[w.par], 16)

            def final_norm(w):
                act.wait_ge(s_nmr, w.n - FIN0 + 1)
                for t in range(T):
                    a = act.activation(fin[:, t, :], fin[:, t, :], ACT.Identity, bias=nmr[:, t:t + 1],
                                       scale=rs[2][:, t:t + 1])
                a.then_inc(s_norm3, 1)

            store_mask(Unit(0, 0))
            exps(Unit(0, 0))
            act.wait_ge(s_col, 48)
            act.wait_ge(s_w[0], 16)

            def split_high(l):
                act.wait_ge(s_w[2 * l], 16)
                for k in range(KD):
                    a = act.activation(w1_hi[:, l, k, :], w1_stage[l][:, k, :], ACT.Identity,
                                       scale=g1_col[:, l, k:k + 1])
                a.then_inc(s_whi, 1)
                act.wait_ge(s_w[2 * l + 1], 16)
                act.activation(w2_hi[:, l, :, :], w2_stage[l], ACT.Identity).then_inc(s_whi, 1)

            split_high(0)
            p_high(Unit(0, 0))
            x_high(Unit(0, 0))
            split_high(1)
            store_mask(Unit(0, 1))
            exps(Unit(0, 1))
            split_high(2)
            n_high(Unit(0, 0))

            def iteration(u, l, mid, l_front, fin_):
                gelu(u, l, 0)
                g_high(u, 0)
                gelu(u, l, 1)
                g_high(u, 1)
                if mid:
                    p_high(u.plus(1))
                gelu(u, l, 2)
                g_high(u, 2)
                if mid:
                    x_high(u.plus(1))
                gelu(u, l, 3)
                g_high(u, 3)
                if fin_:
                    final_norm(u.plus(-2))
                for c in range(4, FC):
                    gelu(u, l, c)
                    g_high(u, c)
                    if c == FC - 2 and l_front == 0:
                        store_mask(u.plus(2))
                if mid:
                    n_high(u.plus(1))
                if l_front is not None:
                    exps(u.plus(2))

            act.wait_ge(s_b1, 1)
            keys = [tuple((layer(u), layer(u + 1) is not None, layer(u + 2), layer(u - 2) == L - 1)
                          for u in (2 * j, 2 * j + 1)) for j in range(PAIRS)]
            for a, b in runs(keys, CUTS):
                with over_pairs(act, a, b) as j:
                    for c in range(2):
                        iteration(Unit(j, c), *keys[a][c])
            for k in (-2, -1):
                final_norm(Unit(PAIRS, k))

        @block.vector
        def _(dve):
            def node_dots(w, l):
                dve.wait_ge(s_x[w.par], 16 * (w.half + 1))
                dve.wait_ge(s_sj, w.n)
                dve.wait_ge(s_bias, w.n)
                for s in (1, 0):
                    for t in range(T):
                        i = (1 - s) * T + t
                        dve.wait_ge(s_dots, 2 * T * w.n + max(0, i - 1))
                        dve.scalar_tensor_tensor(junk[t % 2][:], x_in[w.par][:, t, :], 1.0,
                                                     attn_row[:, l, s * D:(s + 1) * D], ALU.mult, ALU.mult,
                                                     accum_out=dots[:, s, t:t + 1]).then_inc(s_dots, 1)

            def make_mask(w):
                dve.wait_ge(s_adj[w.par], 16 * (w.half + 1))
                if not_first(w):
                    dve.wait_ge(s_smax, w.n - 1)
                dve.wait_ge(s_mstore[w.par], 16 * w.half)
                eye = neg_eye[:].rearrange("p r n -> p (r n)")
                for g in range(G):
                    v = dve.tensor_tensor(mask[w.par][:, g * R:(g + 1) * R, :].rearrange("p r n -> p (r n)"),
                                          adj_in[w.par][:, g * R:(g + 1) * R, :].rearrange("p r n -> p (r n)"),
                                          eye, ALU.is_le)
                v.then_inc(s_conv1, 1)
                dve.wait_ge(s_conv1, w.n + 1)
                m = mask[w.par][:].rearrange("p t n -> p (t n)")
                dve.tensor_scalar(m, m, MASKED, None, ALU.mult).then_inc(s_conv, 1)

            def row_max(w, l):
                dve.wait_ge(s_sj, w.n + 1)
                if l == 0:
                    dve.wait_ge(s_conv, w.n + 1)
                else:
                    dve.wait_ge(s_mask[w.par], 16 * (w.half - PL // 2 + 1))
                dve.wait_ge(s_dots, 2 * T * (w.n + 1))
                dve.wait_ge(s_exp, 2 * T * w.n)
                dve.wait_ge(s_n1, w.n)
                dve.tensor_scalar(cb[:], dots[:, 0, :], attn_b_row[:, l:l + 1], None, ALU.add).then_inc(s_bstep, 1)
                for t in range(T):
                    v = dve.tensor_tensor_reduce(ty[:, t, :], s_bank[:, t // R, :], mask[w.par][:, t, :], 1.0,
                                                 LEAST, ALU.add, ALU.max, smax[:, t:t + 1])
                v.then_inc(s_smax, 1)
                dve.wait_ge(s_smax, w.n + 1)
                dve.wait_ge(s_bstep, 3 * w.n + 1)
                dve.tensor_tensor(zm[:], smax[:], cb[:], ALU.add).then_inc(s_bstep, 1)
                dve.wait_ge(s_bstep, 3 * w.n + 2)
                dve.scalar_tensor_tensor(rmax[:], zm[:], SLOPE, zm[:], ALU.mult, ALU.max).then_inc(s_bstep, 1)
                dve.wait_ge(s_bstep, 3 * w.n + 3)
                dve.tensor_tensor(bias1[:], cb[:], rmax[:], ALU.subtract)
                dve.scalar_tensor_tensor(bias2[:], cb[:], SLOPE, rmax[:], ALU.mult, ALU.subtract).then_inc(s_bias, 1)

            def combine(w):
                for t in range(T):
                    dve.wait_ge(s_exp, 2 * T * w.n + 2 * t + 2)
                    dve.scalar_tensor_tensor(e1[:, t, :], e1[:, t, :], 1.0, e2[:, t, :], ALU.mult, ALU.max,
                                             accum_out=den[:, t:t + 1]).then_inc(s_p, 1)
                dve.wait_ge(s_p, T * (w.n + 1))
                dve.reciprocal(rden[:], den[:]).then_inc(s_rden, 1)

            def p_low(w):
                dve.wait_ge(s_pthi, w.n + 1)
                dve.tensor_tensor(pt_lo[:].rearrange("p g c i -> p (g c i)"), xb[:],
                                  pt_hi[:].rearrange("p g c i -> p (g c i)"), ALU.subtract).then_inc(s_ptlo, 1)

            def x_low(w):
                dve.wait_ge(s_xhi, w.n + 1)
                dve.tensor_tensor(x_lo[:], x_in[w.par][:], x_hi[:], ALU.subtract).then_inc(s_xlo, 1)

            def residual(w):
                dve.wait_ge(s_rden, w.n + 1)
                for t in range(T):
                    if t % R == 0:
                        dve.wait_ge(s_agg, G * w.n + t // R + 1)
                    dve.scalar_tensor_tensor(ty[:, t, :], xb_agg[:, t, :], rden[:, t:t + 1], x_in[w.par][:, t, :],
                                             ALU.mult, ALU.add).then_inc(s_y, 1)

            def statistics(i, src, k, ready, per):
                dve.wait_ge(s_mv[i], k)
                dve.wait_ge((s_n1, s_n2, s_nmr)[i], k)
                for t in range(T):
                    dve.wait_ge(ready, per * k + (t + 1 if per > 1 else 1))
                    dve.bn_stats(bs[i][:, t, :], src[:, t, :]).then_inc(s_bn[i], 1)
                for t in range(T):
                    if t == 0:
                        dve.wait_ge(s_bn[i], T * (k + 1))
                        dve.memset(marker[:], 0.0)
                    v = dve.bn_aggr(mv[i][:, t, :], bs[i][:, t, :])
                v.then_inc(s_mv[i], 1)

            def normalise1(w):
                dve.wait_ge(s_rs[0], w.n + 1)
                if not_first(w):
                    dve.wait_ge(s_z, w.n - 1)
                for t in range(T):
                    v = dve.tensor_scalar(nrm[w.par][:, t, :], ty[:, t, :], mv[0][:, t, 0:1], rs[0][:, t:t + 1],
                                          ALU.subtract, ALU.mult)
                v.then_inc(s_n1, 1)

            def n_low(w):
                dve.wait_ge(s_nthi, w.n + 1)
                dve.tensor_tensor(nt_lo[w.par][:].rearrange("p k n -> p (k n)"), xb[:],
                                  nt_hi[w.par][:].rearrange("p k n -> p (k n)"), ALU.subtract).then_inc(s_ntlo, 1)

            def gl(u, c):
                dve.wait_ge(s_ghi, FC * u.n + c + 1)
                dve.tensor_tensor(g_lo[c % 3][:], g_f[c % 2][:], g_hi[c % 3][:], ALU.subtract).then_inc(s_glo, 1)

            def add_ff(w, prev_last):
                dve.wait_ge(s_f2, FC * (w.n + 1))
                dve.wait_ge(s_hb, w.n + 1)
                if prev_last:
                    dve.wait_ge(s_fin, w.n - FIN0)
                else:
                    v = w.plus(-1)
                    dve.wait_ge(s_xstore[v.par], 16 * (v.half + 1))
                dve.tensor_tensor(zb[:], f2_bank[:], nrm[w.par][:], ALU.add).then_inc(s_z, 1)

            def normalise2(w):
                dve.wait_ge(s_rs[1], w.n + 1)
                for t in range(T):
                    v = dve.tensor_scalar(zb[:, t, :], zb[:, t, :], mv[1][:, t, 0:1], rs[1][:, t:t + 1],
                                          ALU.subtract, ALU.mult)
                v.then_inc(s_n2, 1)

            def final_shift(w):
                dve.wait_ge(s_rs[2], w.n - FIN0 + 1)
                dve.scalar_tensor_tensor(nmr[:], mv[2][:, :, 0], -1.0, rs[2][:], ALU.mult, ALU.mult)\
                   .then_inc(s_nmr, 1)

            def split_low(l):
                dve.wait_ge(s_whi, 2 * l + 1)
                for k in range(KD):
                    v = dve.scalar_tensor_tensor(w1_lo[:, l, k, :], w1_stage[l][:, k, :], g1_col[:, l, k:k + 1],
                                                 w1_hi[:, l, k, :], ALU.mult, ALU.subtract)
                v.then_inc(s_wlo, 1)
                dve.wait_ge(s_whi, 2 * l + 2)
                dve.tensor_tensor(w2_lo[:, l, :, :], w2_stage[l], w2_hi[:, l, :, :], ALU.subtract)\
                   .then_inc(s_wlo, 1)

            dve.wait_ge(s_attn_p, 32)
            dve.wait_ge(s_const, 4)
            w0, w1 = Unit(0, 0), Unit(0, 1)
            node_dots(w0, 0)
            make_mask(w0)
            row_max(w0, 0)
            node_dots(w1, 0)
            make_mask(w1)
            combine(w0)
            split_low(0)
            p_low(w0)
            x_low(w0)
            residual(w0)
            statistics(0, ty, 0, s_y, T)
            dve.wait_ge(s_row, 80)
            dve.tensor_tensor(shift1_row[:], shift1_row[:], b2_row, ALU.add).then_inc(s_shift, 1)
            normalise1(w0)
            row_max(w1, 0)
            split_low(1)
            dve.wait_ge(s_b1ps, 1)
            dve.tensor_tensor(b1_col[:].rearrange("p l c -> p (l c)"), f1_bank[0][:, 0:L * FC],
                              b1_col[:].rearrange("p l c -> p (l c)"), ALU.add).then_inc(s_b1, 1)
            split_low(2)
            n_low(w0)

            def iteration(u, l_front, mid, tail, prev_last, fin_):
                a, b, t = u.plus(1), u.plus(2), u.plus(-1)
                if tail:
                    add_ff(t, prev_last)
                if mid:
                    combine(a)
                if tail:
                    statistics(1, zb, t.n, s_z, 1)
                gl(u, 0)
                if fin_:
                    statistics(2, fin, u.n - 2 - FIN0, s_fin, 1)
                gl(u, 1)
                if mid:
                    p_low(a)
                if tail:
                    normalise2(t)
                gl(u, 2)
                if fin_:
                    final_shift(u.plus(-2))
                if mid:
                    x_low(a)
                gl(u, 3)
                if mid:
                    residual(a)
                    statistics(0, ty, a.n, s_y, T)
                gl(u, 4)
                if l_front is not None:
                    node_dots(b, l_front)
                    if l_front == 0:
                        make_mask(b)
                gl(u, 5)
                if mid:
                    normalise1(a)
                if l_front is not None:
                    row_max(b, l_front)
                gl(u, 6)
                gl(u, 7)
                if mid:
                    n_low(a)

            def key(u):
                return (layer(u + 2), layer(u + 1) is not None, layer(u - 1) is not None,
                        layer(u - 2) == L - 1, layer(u - 2) == L - 1)

            keys = [(key(2 * j), key(2 * j + 1)) for j in range(PAIRS)]
            for a, b in runs(keys, CUTS):
                with over_pairs(dve, a, b) as j:
                    for c in range(2):
                        iteration(Unit(j, c), *keys[a][c])
            end = Unit(PAIRS, 0)
            add_ff(end.plus(-1), True)
            statistics(1, zb, U - 1, s_z, 1)
            statistics(2, fin, U - 2 - FIN0, s_fin, 1)
            normalise2(end.plus(-1))
            final_shift(end.plus(-2))
            statistics(2, fin, U - 1 - FIN0, s_fin, 1)
            final_shift(end.plus(-1))

        @block.gpsimd
        def _(pool):
            def rstd(i, k):
                pool.wait_ge(s_mv[i], k + 1)
                pool.tensor_tensor(ve[i][:], mv[i][:, :, 1], eps_c[:], ALU.add).then_inc(s_ve[i], 1)
                pool.wait_ge(s_ve[i], k + 1)
                pool.tensor_tensor(rs[i][:], ve[i][:], mhalf_c[:], ALU.pow).then_inc(s_rs[i], 1)

            def across(r, l):
                return r[:, l:l + 1, :].to_broadcast([P, T, D])

            def skip_input(u, l):
                b = nrm[u.par][:]
                pool.wait_ge(s_nt, u.n + 1)
                pool.tensor_tensor(b, b, across(g1_row, l), ALU.mult).then_inc(s_hb1, 1)
                pool.wait_ge(s_hb1, u.n + 1)
                pool.tensor_tensor(b, b, across(shift1_row, l), ALU.add).then_inc(s_hb, 1)

            def new_x(w, l):
                pool.wait_ge(s_n2, w.n + 1)
                pool.tensor_tensor(zb[:], zb[:], across(g2_row, l), ALU.mult).then_inc(s_xa1, 1)
                pool.wait_ge(s_xa1, w.n + 1)
                pool.tensor_tensor(zb[:], zb[:], across(beta2_row, l), ALU.add).then_inc(s_xa, 1)

            def final_sum(w):
                pool.wait_ge(s_xa, w.n + 1)
                pool.wait_ge(s_x0, 16 * (w.n - FIN0 + 1))
                pool.wait_ge(s_out, 16 * (w.n - FIN0))
                pool.tensor_tensor(fin[:], zb[:], x0_in[:], ALU.add).then_inc(s_fin, 1)

            pool.memset(ident[:], 1.0)
            pool.memset(neg_eye[:], -1.0)
            pool.memset(eps_c[:], EPS)
            pool.memset(mhalf_c[:], -0.5).then_inc(s_const, 1)
            pool.wait_ge(s_const, 1)
            pool.affine_select(out=ident[:], in_=ident[:], compare_op=ALU.is_equal, fill=0.0, base=0,
                               pattern=[[-1, P]], channel_multiplier=1).then_inc(s_ident, 1)
            for r in range(R):
                v = pool.affine_select(out=neg_eye[:, r, :], in_=neg_eye[:, r, :], compare_op=ALU.is_equal, fill=0.0,
                                       base=r * P, pattern=[[-1, N]], channel_multiplier=1)
            v.then_inc(s_const, 3)

            rstd(0, 0)
            pool.wait_ge(s_row, 80)
            pool.wait_ge(s_shift, 1)

            def iteration(u, l, l_tail, mid, fin_tail, fin_):
                t = u.plus(-1)
                if l_tail is not None:
                    rstd(1, t.n)
                if fin_:
                    rstd(2, u.n - 2 - FIN0)
                if l_tail is not None:
                    new_x(t, l_tail)
                if fin_tail:
                    final_sum(t)
                if mid:
                    rstd(0, u.n + 1)
                if l is not None:
                    skip_input(u, l)

            def key(u):
                return (layer(u), layer(u - 1), layer(u + 1) is not None and layer(u) is not None,
                        layer(u - 1) == L - 1, layer(u - 2) == L - 1)

            keys = [(key(2 * j), key(2 * j + 1)) for j in range(PAIRS + 1)]
            for a, b in runs(keys, CUTS):
                with over_pairs(pool, a, b) as j:
                    for c in range(2):
                        iteration(Unit(j, c), *keys[a][c])


_INS = ['x', 'adj', 'L0_gnn_attn_w', 'L0_gnn_attn_b', 'L0_gnn_W1', 'L0_gnn_b1', 'L0_gnn_W2', 'L0_gnn_b2',
        'L0_gnn_g1', 'L0_gnn_beta1', 'L0_gnn_g2', 'L0_gnn_beta2']


def kernel(**inputs):
    import numpy as _np
    import concourse.bacc as _bacc
    from concourse import mybir as _mybir
    from concourse.bass_utils import run_bass_kernel_spmd as _run

    nc = _bacc.Bacc("TRN2", target_bir_lowering=False, num_devices=1)
    arrays, args = {}, []
    for name in _INS:
        a = _np.ascontiguousarray(inputs[name])
        arrays[f"in_{name}"] = a
        args.append(nc.dram_tensor(f"in_{name}", a.shape, _mybir.dt.from_np(a.dtype), kind="ExternalInput").ap())
    args.append(nc.dram_tensor("out_0", inputs['x'].shape, _mybir.dt.float32, kind="ExternalOutput").ap())
    gnn_kernel(nc, *args)
    r = _run(nc, [arrays], core_ids=[0])
    return r.results[0]["out_0"]
```

```python
from contextlib import ExitStack, nullcontext

import concourse.bass as bass
from concourse import mybir

F32 = mybir.dt.float32
BF16 = mybir.dt.bfloat16
F16 = mybir.dt.float16
I32 = mybir.dt.int32
U8 = mybir.dt.uint8
ALU = mybir.AluOpType
ACT = mybir.ActivationFunctionType

P = 128
EPS = 1e-5
SLOPE = 0.2
MASKED = -3.0e38
LEAST = -3.4e38


class Unit:

    def __init__(self, pair, c):
        self.pair, self.c = pair, c
        self.par = c % 2
        self.half = pair + c // 2
        self.n = 2 * pair + c

    def plus(self, k):
        return Unit(self.pair, self.c + k)


def not_first(w):
    return not (isinstance(w.n, int) and w.n == 0)


def runs(keys, cuts):
    a = 0
    for b in range(1, len(keys) + 1):
        if b == len(keys) or keys[b] != keys[a] or b in cuts:
            yield a, b
            a = b


def over_pairs(eng, a, b):
    return eng.Fori(a, b) if b - a > 1 else nullcontext(a)


def gnn_kernel(nc, x, adj, attn_w, attn_b, W1, b1, W2, b2, g1, beta1, g2, beta2, out):
    B, N, D = x.shape
    L, _, F = W1.shape
    R = N // P
    G = 2
    T = G * R
    TOK = T * P
    KD = D // P
    FC = F // P
    PL = B // G
    U = L * PL
    PAIRS = U // 2
    TD = T * D
    NB1 = 3

    def layer(u):
        return u // PL if 0 <= u < U else None

    x_d = x.rearrange("(u g) (r q) d -> u q g r d", g=G, q=P)
    out_d = out.rearrange("(u g) (r q) d -> u q g r d", g=G, q=P)
    adj_d = adj.rearrange("(u g) (r q) j -> u q g r j", g=G, q=P)
    MASK_BYTES = P * T * N * 2
    mask_store = nc.dram_tensor("mask_store", [PL * MASK_BYTES], U8, kind="Internal").ap()

    with ExitStack() as ctx:
        def sb(name, shape, dt):
            return ctx.enter_context(nc.sbuf_tensor(name, shape, dt))

        def psum(name, shape, dt):
            return ctx.enter_context(nc.psum_tensor(name, shape, dt))

        def sem(name):
            return ctx.enter_context(nc.semaphore(name))

        x_store = sb("x_store", [P, PL * TD], F32)
        w_stage = [x_store[:, l * KD * F:(l + 1) * KD * F] for l in range(2 * L)]
        w1_stage = [w_stage[2 * l].rearrange("p (k f) -> p k f", k=KD) for l in range(L)]
        w2_stage = [w_stage[2 * l + 1].rearrange("p (c d) -> p c d", c=FC) for l in range(L)]
        w1_hi = sb("w1_hi", [P, L, KD, F], BF16)
        w1_lo = sb("w1_lo", [P, L, KD, F], BF16)
        w2_hi = sb("w2_hi", [P, L, FC, D], BF16)
        w2_lo = sb("w2_lo", [P, L, FC, D], BF16)
        g1_col = sb("g1_col", [P, L, KD], F32)
        beta1_col = sb("beta1_col", [P, L, KD], F32)
        b1_col = sb("b1_col", [P, L, FC], F32)
        g1_row = sb("g1_row", [P, L, D], F32)
        shift1_row = sb("shift1_row", [P, L, D], F32)
        g2_row = sb("g2_row", [P, L, D], F32)
        beta2_row = sb("beta2_row", [P, L, D], F32)
        attn_row = sb("attn_row", [P, L, 2 * D], F32)
        attn_b_row = sb("attn_b_row", [P, L], F32)
        ident = sb("ident", [P, P], F32)
        neg_eye = sb("neg_eye", [P, R, N], F32)
        eps_c = sb("eps_c", [P, T], F32)
        mhalf_c = sb("mhalf_c", [P, T], F32)

        x_in = [sb(f"x_in{i}", [P, T, D], F32) for i in range(2)]
        stage = [sb(f"stage{i}", [P, T, D], F32) for i in range(2)]
        adj_in = [s[:].bitcast(I32) for s in stage]
        mask = [sb(f"mask{i}", [P, T, N], BF16) for i in range(2)]
        junk = [sb(f"junk{i}", [P, D], F32) for i in range(2)]
        ty = sb("ty", [P, T, D], F32)
        e1 = sb("e1", [P, T, N], F32)
        e2 = sb("e2", [P, T, N], F32)
        pt_hi = sb("pt_hi", [P, G, R, N], F16)
        pt_lo = sb("pt_lo", [P, G, R, N], F16)
        x_hi = sb("x_hi", [P, T, D], BF16)
        x_lo = sb("x_lo", [P, T, D], BF16)
        nrm = [sb(f"nrm{i}", [P, T, D], F32) for i in range(2)]
        nt_hi = [sb(f"nt_hi{i}", [P, KD, TOK], F16) for i in range(2)]
        nt_lo = [sb(f"nt_lo{i}", [P, KD, TOK], F16) for i in range(2)]
        g_f = [sb(f"g_f{i}", [P, TOK], F32) for i in range(2)]
        g_hi = [sb(f"g_hi{i}", [P, TOK], BF16) for i in range(3)]
        g_lo = [sb(f"g_lo{i}", [P, TOK], BF16) for i in range(3)]
        zb = sb("zb", [P, T, D], F32)

        b2_row = zb[:, 0:L, :]

        dots = sb("dots", [P, 2, T], F32)
        smax = sb("smax", [P, T], F32)
        cb = sb("cb", [P, T], F32)
        zm = sb("zm", [P, T], F32)
        rmax = sb("rmax", [P, T], F32)
        bias1 = sb("bias1", [P, T], F32)
        bias2 = sb("bias2", [P, T], F32)
        den = sb("den", [P, T], F32)
        rden = [sb(f"rden{i}", [P, T], F32) for i in range(2)]
        bs = [sb(f"bs{i}", [P, T, 6], F32) for i in range(3)]
        mv = [sb(f"mv{i}", [P, T, 2], F32) for i in range(3)]
        rs = [sb(f"rs{i}", [P, T], F32) for i in range(3)]
        ve = [sb(f"ve{i}", [P, T], F32) for i in range(3)]
        marker = sb("marker", [P, 1], F32)
        nmr = sb("nmr", [P, T], F32)

        s_bank = psum("s_bank", [P, G, N], F32)
        xb = psum("xb", [P, 2 * 512], F32)
        f1_bank = [psum(f"f1_bank{i}", [P, TOK], F32) for i in range(NB1)]
        f2_bank = psum("f2_bank", [P, T, D], F32)
        xb_pt = xb[:].rearrange("p (g c i) -> p g c i", g=G, c=R)
        xb_agg = xb[:].rearrange("p (t d) -> p t d", t=T)
        xb_nt = xb[:].rearrange("p (k n) -> p k n", k=KD)

        s_x = [sem(f"s_x{i}") for i in range(2)]
        s_adj = [sem(f"s_adj{i}") for i in range(2)]
        s_mask = [sem(f"s_mask{i}") for i in range(2)]
        s_mstore = [sem(f"s_mstore{i}") for i in range(2)]
        s_xstore = [sem(f"s_xstore{i}") for i in range(2)]
        s_x0 = [sem(f"s_x0in{i}") for i in range(2)]
        s_out = [sem(f"s_out{i}") for i in range(2)]
        s_attn_p = sem("s_attn_p")
        s_col = sem("s_col")
        s_row = sem("s_row")
        s_w = [sem(f"s_w{i}") for i in range(2 * L)]
        s_const = sem("s_const")
        s_ident = sem("s_ident")
        s_whi = sem("s_whi")
        s_wlo = sem("s_wlo")
        s_b1ps = sem("s_b1ps")
        s_b1 = sem("s_b1")
        s_shift = sem("s_shift")
        s_dots = sem("s_dots")
        s_conv1 = sem("s_conv1")
        s_conv = sem("s_conv")
        s_sj = sem("s_sj")
        s_smax = sem("s_smax")
        s_bstep = sem("s_bstep")
        s_bias = sem("s_bias")
        s_exp = sem("s_exp")
        s_p = sem("s_p")
        s_rden = sem("s_rden")
        s_pt = sem("s_pt")
        s_pthi = sem("s_pthi")
        s_ptlo = sem("s_ptlo")
        s_xhi = sem("s_xhi")
        s_xlo = sem("s_xlo")
        s_agg = sem("s_agg")
        s_y = sem("s_y")
        s_bn = [sem(f"s_bn{i}") for i in range(3)]
        s_mv = [sem(f"s_mv{i}") for i in range(3)]
        s_ve = [sem(f"s_ve{i}") for i in range(3)]
        s_rs = [sem(f"s_rs{i}") for i in range(3)]
        s_n1 = sem("s_n1")
        s_nt = sem("s_nt")
        s_nthi = sem("s_nthi")
        s_ntlo = sem("s_ntlo")
        s_f1 = sem("s_f1")
        s_gelu = sem("s_gelu")
        s_ghi = sem("s_ghi")
        s_glo = sem("s_glo")
        s_f2 = sem("s_f2")
        s_hb1 = sem("s_hb1")
        s_hb = sem("s_hb")
        s_z = sem("s_z")
        s_n2 = sem("s_n2")
        s_xa1 = sem("s_xa1")
        s_xa = sem("s_xa")
        s_fin = sem("s_fin")
        s_nmr = sem("s_nmr")
        s_norm3 = sem("s_norm3")

        FIN0 = (L - 1) * PL
        CUTS = (1, 2, FIN0 // 2 + 1, FIN0 // 2 + 2)

        def stored_mask(at):
            return mask_store[bass.ds(at, MASK_BYTES)].rearrange("(q b) -> q b", q=P)

        def mask_bytes(w):
            return mask[w.par][:].rearrange("q t d -> q (t d)").bitcast(U8)

        def split_w2_low(eng, l):
            eng.wait_ge(s_whi, 2 * l + 2)
            eng.tensor_tensor(w2_lo[:, l, :, :], w2_stage[l], w2_hi[:, l, :, :], ALU.subtract).then_inc(s_wlo, 1)

        def w1_beside(u):
            return u // 2 + 1 if u in range(0, 2 * (L - 1), 2) else None

        def w2_beside(u):
            return u // 2 + 1 if u in range(1, 2 * (L - 1), 2) else None

        block = ctx.enter_context(nc.Block())

        @block.sync
        def _(sp):
            def load_x(w, l, p):
                if l == 0:
                    src = x_d[p]
                else:
                    sp.wait_ge(s_xstore[w.par], 16 * (w.half - PL // 2 + 1))
                    src = x_store[:, bass.ts(p, TD)].rearrange("q (t d) -> q t d", t=T)
                dst = x_in[w.par][:].rearrange("q (g r) d -> q g r d", g=G) if l == 0 else x_in[w.par][:]
                sp.dma_start(dst, src).then_inc(s_x[w.par], 16)

            def load_adj(w, p):
                dst = adj_in[w.par].rearrange("q (g r) d -> q g r d", g=G)
                sp.dma_start(dst, adj_d[p]).then_inc(s_adj[w.par], 16)

            def load_mask(w, l, at):
                if l == 1:
                    sp.wait_ge(s_mstore[w.par], 16 * (PL // 2))
                sp.wait_ge(s_smax, w.n - 1)
                sp.dma_start(mask_bytes(w), stored_mask(at)).then_inc(s_mask[w.par], 16)

            def row(dst, src, s):
                sp.dma_start(dst, src).then_inc(s, 16)

            def load_w1(l):
                sp.dma_start(w1_stage[l], W1[l].rearrange("(k p) f -> p k f", p=P)).then_inc(s_w[2 * l], 16)

            def load_w2(l):
                sp.dma_start(w2_stage[l], W2[l].rearrange("(c p) d -> p c d", p=P)).then_inc(s_w[2 * l + 1], 16)

            u0 = Unit(0, 0)
            load_x(u0, 0, 0)
            row(attn_row[:], attn_w.partition_broadcast(P), s_attn_p)
            row(attn_b_row[:], attn_b.partition_broadcast(P), s_attn_p)
            load_adj(u0, 0)
            load_x(u0.plus(1), 0, 1)
            load_adj(u0.plus(1), 1)
            with nc.allow_non_contiguous_dma(reason="a few parameters, feature on the partition"):
                row(g1_col[:], g1.rearrange("l (k p) -> p l k", p=P), s_col)
                row(beta1_col[:], beta1.rearrange("l (k p) -> p l k", p=P), s_col)
                row(b1_col[:], b1.rearrange("l (c p) -> p l c", p=P), s_col)
            for l in range(L):
                load_w1(l)
            load_w2(0)
            row(g1_row[:], g1.partition_broadcast(P), s_row)
            row(shift1_row[:], beta1.partition_broadcast(P), s_row)
            row(b2_row, b2.partition_broadcast(P), s_row)
            row(g2_row[:], g2.partition_broadcast(P), s_row)
            row(beta2_row[:], beta2.partition_broadcast(P), s_row)
            for k in range(2):
                sp.wait_ge(s_conv, k + 1)
                load_adj(u0.plus(k + 2), k + 2)
            sp.wait_ge(s_y, T)
            load_x(u0.plus(2), 0, 2)
            for l in range(1, L):
                load_w2(l)
            sp.wait_ge(s_wlo, 2)
            sp.wait_ge(s_whi, 2)
            sp.wait_ge(s_b1ps, 1)

            def step_key(u):
                return (layer(u - 1), layer(u + 3), layer(u + 4), layer(u - 2))

            def step(u, key):
                l_prev, l_x, l_next, l_fin = key
                last = L - 1

                places = {}
                for k, l in ((-1, l_prev), (-2, l_fin), (3, l_x), (4, l_next)):
                    if l is not None:
                        v = u.n + k - PL * l
                        if k == 4 and l > 0:
                            v = v * MASK_BYTES
                        places[k, l] = v if isinstance(v, int) else sp.snap(v)

                def at(k, l):
                    return places[k, l]
                if l_prev == last:
                    v = u.plus(-1)
                    sp.wait_ge(s_out[v.par], 16 * (v.half - FIN0 // 2))
                    sp.dma_start(stage[v.par][:].rearrange("q (g r) d -> q g r d", g=G), x_d[at(-1, last)])\
                      .then_inc(s_x0[v.par], 16)
                elif l_prev is not None:
                    v = u.plus(-1)
                    sp.wait_ge(s_xa, v.n + 1)
                    sp.dma_start(x_store[:, bass.ts(at(-1, l_prev), TD)].rearrange("q (t d) -> q t d", t=T),
                                 zb[:]).then_inc(s_xstore[v.par], 16)
                if l_x is not None:
                    v = u.plus(3)
                    sp.wait_ge(s_y, T * (v.n - 1))
                    load_x(v, l_x, at(3, l_x))
                if l_next == 0:
                    v = u.plus(4)
                    sp.wait_ge(s_conv, v.n - 1)
                    load_adj(v, at(4, 0))
                elif l_next is not None:
                    load_mask(u.plus(4), l_next, at(4, l_next))
                if l_fin == last:
                    v = u.plus(-2)
                    sp.wait_ge(s_norm3, v.n - FIN0 + 1)
                    sp.dma_start(out_d[at(-2, last)], stage[v.par][:].rearrange("q (g r) d -> q g r d", g=G))\
                      .then_inc(s_out[v.par], 16)

            keys = [(step_key(2 * j), step_key(2 * j + 1)) for j in range(PAIRS + 1)]
            for a, b in runs(keys, CUTS):
                if a == 2:
                    sp.wait_ge(s_wlo, 2 * L)
                    sp.wait_ge(s_whi, 2 * L)
                with over_pairs(sp, a, b) as j:
                    for c in range(2):
                        step(Unit(j, c), keys[a][c])
            for i in range(2):
                sp.wait_ge(s_out[i], 16 * (PL // 2))

        @block.tensor
        def _(pe):
            def scores(w):
                pe.wait_ge(s_dots, 2 * T * (w.n + 1))
                pe.wait_ge(s_smax, w.n)
                for t in range(T):
                    mm = pe.transpose(s_bank[:, t // R, (t % R) * P:(t % R + 1) * P],
                                      dots[:, 1, t:t + 1].to_broadcast([P, P]), ident[:])
                mm.then_inc(s_sj, 1)

            def p_transposes(w):
                pe.wait_ge(s_p, T * (w.n + 1))
                pe.wait_ge(s_ntlo, w.n)
                for t in range(T):
                    for c in range(R):
                        mm = pe.transpose(xb_pt[:, t // R, c, (t % R) * P:(t % R + 1) * P],
                                          e1[:, t, c * P:(c + 1) * P], ident[:])
                mm.then_inc(s_pt, 1)

            def aggregate(w):
                pe.wait_ge(s_ptlo, w.n + 1)
                pe.wait_ge(s_xlo, w.n + 1)
                for t in range(T):
                    g, r = t // R, t % R
                    parts = [(a, b, c) for c in range(R) for a, b in ((pt_hi, x_hi), (pt_hi, x_lo), (pt_lo, x_hi))]
                    for i, (a, b, c) in enumerate(parts):
                        mm = pe.matmul(xb_agg[:, t, :], a[:, g, c, r * P:(r + 1) * P], b[:, g * R + c, :],
                                       start=(i == 0), stop=(i == len(parts) - 1))
                    if r == R - 1:
                        mm.then_inc(s_agg, 1)

            def n_transposes(w):
                pe.wait_ge(s_n1, w.n + 1)
                for k in range(KD):
                    for t in range(T):
                        mm = pe.transpose(xb_nt[:, k, t * P:(t + 1) * P],
                                          nrm[w.par][:, t, k * P:(k + 1) * P], ident[:])
                mm.then_inc(s_nt, 1)

            def hidden(u, l, c):
                if c == 0:
                    pe.wait_ge(s_ntlo, u.n + 1)
                pe.wait_ge(s_gelu, FC * u.n + max(0, c - NB1 + 1))
                parts = [(a, b, k) for k in range(KD) for a, b in ((w1_hi, nt_hi), (w1_hi, nt_lo), (w1_lo, nt_hi))]
                for i, (a, b, k) in enumerate(parts):
                    mm = pe.matmul(f1_bank[c % NB1][:], a[:, l, k, c * P:(c + 1) * P], b[u.par][:, k, :],
                                   start=(i == 0), stop=(i == len(parts) - 1))
                mm.then_inc(s_f1, 1)

            def project(u, l, c):
                pe.wait_ge(s_glo, FC * u.n + c + 1)
                if c == 0:
                    pe.wait_ge(s_z, u.n)
                for t in range(T):
                    for i, (a, b) in enumerate(((g_hi, w2_hi), (g_hi, w2_lo), (g_lo, w2_hi))):
                        mm = pe.matmul(f2_bank[:, t, :], a[c % 3][:, t * P:(t + 1) * P], b[:, l, c, :],
                                       start=(c == 0 and i == 0 and t % 2 == 0), stop=(c == FC - 1 and i == 2),
                                       skip_group_check=True)
                mm.then_inc(s_f2, 1)

            def shift_through_w1(l):
                pe.wait_ge(s_w[2 * l], 16)
                for c in range(FC):
                    for k in range(KD):
                        mm = pe.matmul(f1_bank[0][:, l * FC + c:l * FC + c + 1], w1_stage[l][:, k, c * P:(c + 1) * P],
                                       beta1_col[:, l, k:k + 1], start=(k == 0), stop=(k == KD - 1))
                mm.then_inc(s_b1ps, 1)

            pe.wait_ge(s_ident, 1)
            scores(Unit(0, 0))
            scores(Unit(0, 1))
            p_transposes(Unit(0, 0))
            pe.wait_ge(s_col, 48)
            shift_through_w1(0)
            aggregate(Unit(0, 0))
            shift_through_w1(1)
            n_transposes(Unit(0, 0))
            shift_through_w1(2)
            scores(Unit(0, 2))
            pe.wait_ge(s_b1, 1)
            pe.wait_ge(s_wlo, 2)
            pe.wait_ge(s_whi, 2)

            def iteration(u, l, mid, front):
                hidden(u, l, 0)
                if mid:
                    p_transposes(u.plus(1))
                hidden(u, l, 1)
                hidden(u, l, 2)
                project(u, l, 0)
                if mid:
                    aggregate(u.plus(1))
                hidden(u, l, 3)
                project(u, l, 1)
                hidden(u, l, 4)
                project(u, l, 2)
                hidden(u, l, 5)
                project(u, l, 3)
                hidden(u, l, 6)
                project(u, l, 4)
                hidden(u, l, 7)
                if mid:
                    n_transposes(u.plus(1))
                project(u, l, 5)
                project(u, l, 6)
                if front:
                    scores(u.plus(3))
                project(u, l, 7)

            keys = [tuple((layer(u), layer(u + 1) is not None, layer(u + 3) is not None)
                          for u in (2 * j, 2 * j + 1)) for j in range(PAIRS)]
            for a, b in runs(keys, CUTS):
                if a == PL // 2:
                    pe.wait_ge(s_wlo, 2 * L)
                    pe.wait_ge(s_whi, 2 * L)
                with over_pairs(pe, a, b) as j:
                    for c in range(2):
                        iteration(Unit(j, c), *keys[a][c])

        @block.scalar
        def _(act):
            def exps(w):
                act.wait_ge(s_bias, w.n + 1)
                act.wait_ge(s_pt, w.n)
                for t in range(T):
                    act.activation(e1[:, t, :], ty[:, t, :], ACT.Exp, bias=bias1[:, t:t + 1]).then_inc(s_exp, 1)
                    act.activation(e2[:, t, :], ty[:, t, :], ACT.Exp, bias=bias2[:, t:t + 1],
                                   scale=SLOPE).then_inc(s_exp, 1)

            def p_high(w):
                act.wait_ge(s_pt, w.n + 1)
                act.wait_ge(s_agg, G * w.n)
                act.activation(pt_hi[:].rearrange("p g c i -> p (g c i)"), xb[:], ACT.Identity).then_inc(s_pthi, 1)

            def x_high(w):
                act.wait_ge(s_x[w.par], 16 * (w.half + 1))
                act.wait_ge(s_agg, G * w.n)
                act.activation(x_hi[:], x_in[w.par][:], ACT.Identity).then_inc(s_xhi, 1)

            def n_high(w):
                act.wait_ge(s_nt, w.n + 1)
                act.activation(nt_hi[w.par][:].rearrange("p k n -> p (k n)"), xb[:], ACT.Identity)\
                   .then_inc(s_nthi, 1)

            def gelu(u, l, c):
                act.wait_ge(s_f1, FC * u.n + c + 1)
                act.wait_ge(s_glo, FC * u.n + max(0, c - 1))
                act.activation(g_f[c % 2][:], f1_bank[c % NB1][:], ACT.Gelu, bias=b1_col[:, l, c:c + 1])\
                   .then_inc(s_gelu, 1)

            def g_high(u, c):
                act.wait_ge(s_gelu, FC * u.n + c + 1)
                act.wait_ge(s_f2, FC * u.n + max(0, c - 2))
                act.activation(g_hi[c % 3][:], g_f[c % 2][:], ACT.Identity).then_inc(s_ghi, 1)

            def store_mask(w):
                act.wait_ge(s_conv, w.n + 1)
                act.dma_start(stored_mask(w.n * MASK_BYTES), mask_bytes(w)).then_inc(s_mstore[w.par], 16)

            def final_norm(w):
                act.wait_ge(s_nmr, w.n - FIN0 + 1)
                for t in range(T):
                    a = act.activation(stage[w.par][:, t, :], stage[w.par][:, t, :], ACT.Identity, bias=nmr[:, t:t + 1],
                                       scale=rs[2][:, t:t + 1])
                a.then_inc(s_norm3, 1)

            def split_w1_high(l):
                act.wait_ge(s_w[2 * l], 16)
                for k in range(KD):
                    a = act.activation(w1_hi[:, l, k, :], w1_stage[l][:, k, :], ACT.Identity,
                                       scale=g1_col[:, l, k:k + 1])
                a.then_inc(s_whi, 1)

            def split_w2_high(l):
                act.wait_ge(s_w[2 * l + 1], 16)
                act.activation(w2_hi[:, l, :, :], w2_stage[l], ACT.Identity).then_inc(s_whi, 1)

            w0, w1 = Unit(0, 0), Unit(0, 1)
            store_mask(w0)
            exps(w0)
            x_high(w0)
            p_high(w0)
            act.wait_ge(s_col, 48)
            split_w1_high(0)
            store_mask(w1)
            exps(w1)
            split_w2_high(0)
            n_high(w0)
            x_high(w1)
            store_mask(Unit(0, 2))

            def iteration(u, l, mid, exp_, l_front, fin_, w1_l, w2_l):
                gelu(u, l, 0)
                g_high(u, 0)
                if mid:
                    p_high(u.plus(1))
                for c in (1, 2):
                    gelu(u, l, c)
                    g_high(u, c)
                if exp_:
                    exps(u.plus(2))
                for c in range(3, FC):
                    gelu(u, l, c)
                    g_high(u, c)
                    if c == 4:
                        if exp_:
                            x_high(u.plus(2))
                    if w1_l and c == 4:
                        split_w1_high(w1_l)
                    if w2_l and c == 4:
                        split_w2_high(w2_l)
                    if c == FC - 2 and l_front == 0:
                        store_mask(u.plus(3))
                    if c == FC - 2 and fin_:
                        final_norm(u.plus(-2))
                if mid:
                    n_high(u.plus(1))

            act.wait_ge(s_b1, 1)
            keys = [tuple((layer(u), layer(u + 1) is not None, layer(u + 2) is not None, layer(u + 3), layer(u - 2) == L - 1,
                           w1_beside(u), w2_beside(u)) for u in (2 * j, 2 * j + 1)) for j in range(PAIRS)]
            for a, b in runs(keys, CUTS):
                with over_pairs(act, a, b) as j:
                    for c in range(2):
                        iteration(Unit(j, c), *keys[a][c])
            for k in (-2, -1):
                final_norm(Unit(PAIRS, k))

        @block.vector
        def _(dve):
            def node_dots(w, l, which=(1, 0)):
                if 1 in which:
                    dve.wait_ge(s_x[w.par], 16 * (w.half + 1))
                    dve.wait_ge(s_sj, w.n)
                    dve.wait_ge(s_bias, w.n)
                for s in which:
                    for t in range(T):
                        i = (1 - s) * T + t
                        dve.wait_ge(s_dots, 2 * T * w.n + max(0, i - 1))
                        dve.scalar_tensor_tensor(junk[t % 2][:], x_in[w.par][:, t, :], 1.0,
                                                     attn_row[:, l, s * D:(s + 1) * D], ALU.mult, ALU.mult,
                                                     accum_out=dots[:, s, t:t + 1]).then_inc(s_dots, 1)

            def make_mask(w):
                dve.wait_ge(s_adj[w.par], 16 * (w.half + 1))
                if not_first(w):
                    dve.wait_ge(s_smax, w.n - 1)
                dve.wait_ge(s_mstore[w.par], 16 * w.half)
                eye = neg_eye[:].rearrange("p r n -> p (r n)")
                for g in range(G):
                    v = dve.tensor_tensor(mask[w.par][:, g * R:(g + 1) * R, :].rearrange("p r n -> p (r n)"),
                                          adj_in[w.par][:, g * R:(g + 1) * R, :].rearrange("p r n -> p (r n)"),
                                          eye, ALU.is_le)
                v.then_inc(s_conv1, 1)
                dve.wait_ge(s_conv1, w.n + 1)
                m = mask[w.par][:].rearrange("p t n -> p (t n)")
                dve.tensor_scalar(m, m, MASKED, None, ALU.mult).then_inc(s_conv, 1)

            def row_max(w, l):
                dve.wait_ge(s_sj, w.n + 1)
                if l == 0:
                    dve.wait_ge(s_conv, w.n + 1)
                else:
                    dve.wait_ge(s_mask[w.par], 16 * (w.half - PL // 2 + 1))
                dve.wait_ge(s_dots, 2 * T * (w.n + 1))
                dve.wait_ge(s_exp, 2 * T * w.n)
                dve.tensor_scalar(cb[:], dots[:, 0, :], attn_b_row[:, l:l + 1], None, ALU.add).then_inc(s_bstep, 1)
                for t in range(T):
                    v = dve.tensor_tensor_reduce(ty[:, t, :], s_bank[:, t // R, :], mask[w.par][:, t, :], 1.0,
                                                 LEAST, ALU.add, ALU.max, smax[:, t:t + 1])
                v.then_inc(s_smax, 1)
                dve.wait_ge(s_smax, w.n + 1)
                dve.wait_ge(s_bstep, 3 * w.n + 1)
                dve.tensor_tensor(zm[:], smax[:], cb[:], ALU.add).then_inc(s_bstep, 1)
                dve.wait_ge(s_bstep, 3 * w.n + 2)
                dve.scalar_tensor_tensor(rmax[:], zm[:], SLOPE, zm[:], ALU.mult, ALU.max).then_inc(s_bstep, 1)
                dve.wait_ge(s_bstep, 3 * w.n + 3)
                dve.tensor_tensor(bias1[:], cb[:], rmax[:], ALU.subtract)
                dve.scalar_tensor_tensor(bias2[:], cb[:], SLOPE, rmax[:], ALU.mult, ALU.subtract).then_inc(s_bias, 1)

            def combine(w):
                for t in range(T):
                    dve.wait_ge(s_exp, 2 * T * w.n + 2 * t + 2)
                    dve.scalar_tensor_tensor(e1[:, t, :], e1[:, t, :], 1.0, e2[:, t, :], ALU.mult, ALU.max,
                                             accum_out=den[:, t:t + 1]).then_inc(s_p, 1)
                dve.wait_ge(s_p, T * (w.n + 1))
                dve.reciprocal(rden[w.par][:], den[:]).then_inc(s_rden, 1)

            def p_low(w):
                dve.wait_ge(s_pthi, w.n + 1)
                dve.tensor_tensor(pt_lo[:].rearrange("p g c i -> p (g c i)"), xb[:],
                                  pt_hi[:].rearrange("p g c i -> p (g c i)"), ALU.subtract).then_inc(s_ptlo, 1)

            def residual(w):
                if not_first(w):
                    dve.wait_ge(s_z, w.n - 1)
                dve.wait_ge(s_rden, w.n + 1)
                for t in range(T):
                    if t % R == 0:
                        dve.wait_ge(s_agg, G * w.n + t // R + 1)
                    dve.scalar_tensor_tensor(nrm[w.par][:, t, :], xb_agg[:, t, :], rden[w.par][:, t:t + 1],
                                             x_in[w.par][:, t, :],
                                             ALU.mult, ALU.add).then_inc(s_y, 1)

            def bn_halves(i, src, k, ready, per):
                dve.wait_ge(s_mv[i], k)
                for t in range(T):
                    dve.wait_ge(ready, per * k + (t + 1 if per > 1 else 1))
                    dve.bn_stats(bs[i][:, t, :], src[:, t, :]).then_inc(s_bn[i], 1)

            def mean_variance(i, k):
                dve.wait_ge((s_n1, s_n2, s_nmr)[i], k)
                dve.wait_ge(s_bn[i], T * (k + 1))
                dve.memset(marker[:], 0.0)
                for t in range(T):
                    v = dve.bn_aggr(mv[i][:, t, :], bs[i][:, t, :])
                v.then_inc(s_mv[i], 1)

            def normalise1(w):
                dve.wait_ge(s_rs[0], w.n + 1)
                for t in range(T):
                    v = dve.tensor_scalar(nrm[w.par][:, t, :], nrm[w.par][:, t, :], mv[0][:, t, 0:1], rs[0][:, t:t + 1],
                                          ALU.subtract, ALU.mult)
                v.then_inc(s_n1, 1)

            def n_low(w):
                dve.wait_ge(s_nthi, w.n + 1)
                dve.tensor_tensor(nt_lo[w.par][:].rearrange("p k n -> p (k n)"), xb[:],
                                  nt_hi[w.par][:].rearrange("p k n -> p (k n)"), ALU.subtract).then_inc(s_ntlo, 1)

            def gl(u, c):
                dve.wait_ge(s_ghi, FC * u.n + c + 1)
                dve.tensor_tensor(g_lo[c % 3][:], g_f[c % 2][:], g_hi[c % 3][:], ALU.subtract).then_inc(s_glo, 1)

            def add_ff(w, prev_last):
                dve.wait_ge(s_f2, FC * (w.n + 1))
                dve.wait_ge(s_hb, w.n + 1)
                if prev_last:
                    dve.wait_ge(s_fin, w.n - FIN0)
                else:
                    v = w.plus(-1)
                    dve.wait_ge(s_xstore[v.par], 16 * (v.half + 1))
                dve.tensor_tensor(zb[:], f2_bank[:], nrm[w.par][:], ALU.add).then_inc(s_z, 1)

            def normalise2(w):
                dve.wait_ge(s_rs[1], w.n + 1)
                for t in range(T):
                    v = dve.tensor_scalar(zb[:, t, :], zb[:, t, :], mv[1][:, t, 0:1], rs[1][:, t:t + 1],
                                          ALU.subtract, ALU.mult)
                v.then_inc(s_n2, 1)

            def final_shift(w):
                dve.wait_ge(s_rs[2], w.n - FIN0 + 1)
                dve.scalar_tensor_tensor(nmr[:], mv[2][:, :, 0], -1.0, rs[2][:], ALU.mult, ALU.mult)\
                   .then_inc(s_nmr, 1)

            def split_w1_low(l):
                dve.wait_ge(s_whi, 2 * l + 1)
                for k in range(KD):
                    v = dve.scalar_tensor_tensor(w1_lo[:, l, k, :], w1_stage[l][:, k, :], g1_col[:, l, k:k + 1],
                                                 w1_hi[:, l, k, :], ALU.mult, ALU.subtract)
                v.then_inc(s_wlo, 1)

            dve.wait_ge(s_attn_p, 32)
            dve.wait_ge(s_const, 4)
            w0, w1, w2 = Unit(0, 0), Unit(0, 1), Unit(0, 2)
            node_dots(w0, 0)
            make_mask(w0)
            row_max(w0, 0)
            node_dots(w1, 0)
            combine(w0)
            make_mask(w1)
            row_max(w1, 0)
            p_low(w0)
            split_w1_low(0)
            residual(w0)
            bn_halves(0, nrm[0], 0, s_y, T)
            mean_variance(0, 0)
            combine(w1)
            normalise1(w0)
            split_w2_low(dve, 0)
            n_low(w0)
            node_dots(w2, 0)
            make_mask(w2)
            dve.wait_ge(s_b1ps, L)
            b1 = b1_col[:].rearrange("p l c -> p (l c)")
            dve.tensor_tensor(b1, f1_bank[0][:, 0:L * FC], b1, ALU.add).then_inc(s_b1, 1)
            row_max(w2, 0)

            def iteration(u, l_front, exp_, mid, tail, prev_last, fin_, split):
                a, b, f, t = u.plus(1), u.plus(2), u.plus(3), u.plus(-1)
                if tail:
                    add_ff(t, prev_last)
                gl(u, 0)
                if mid:
                    p_low(a)
                if tail:
                    bn_halves(1, zb, t.n, s_z, 1)
                gl(u, 1)
                if tail:
                    mean_variance(1, t.n)
                gl(u, 2)
                if tail:
                    normalise2(t)
                if mid:
                    residual(a)
                    bn_halves(0, nrm[a.par], a.n, s_y, T)
                if exp_:
                    combine(b)
                gl(u, 3)
                if mid:
                    mean_variance(0, a.n)
                if fin_:
                    bn_halves(2, stage[u.par], u.n - 2 - FIN0, s_fin, 1)
                gl(u, 4)
                if fin_:
                    mean_variance(2, u.n - 2 - FIN0)
                if l_front == 0:
                    make_mask(f)
                if split:
                    split_w1_low(split)
                gl(u, 5)
                if mid:
                    normalise1(a)
                if l_front is not None:
                    node_dots(f, l_front, (1,))
                if fin_:
                    final_shift(u.plus(-2))
                gl(u, 6)
                if l_front is not None:
                    node_dots(f, l_front, (0,))
                gl(u, 7)
                if mid:
                    n_low(a)
                if l_front is not None:
                    row_max(f, l_front)

            def key(u):
                return (layer(u + 3), layer(u + 2) is not None, layer(u + 1) is not None,
                        layer(u - 1) is not None, layer(u - 2) == L - 1, layer(u - 2) == L - 1,
                        w1_beside(u))

            keys = [(key(2 * j), key(2 * j + 1)) for j in range(PAIRS)]
            for a, b in runs(keys, CUTS):
                with over_pairs(dve, a, b) as j:
                    for c in range(2):
                        iteration(Unit(j, c), *keys[a][c])
            end = Unit(PAIRS, 0)
            w, v = end.plus(-1), end.plus(-2)
            add_ff(w, True)
            bn_halves(1, zb, U - 1, s_z, 1)
            mean_variance(1, U - 1)
            bn_halves(2, stage[v.par], v.n - FIN0, s_fin, 1)
            mean_variance(2, v.n - FIN0)
            normalise2(w)
            final_shift(v)
            dve.wait_ge(s_n2, U)
            dve.tensor_tensor(zb[:], zb[:], g2_row[:, L - 1:L, :].to_broadcast([P, T, D]), ALU.mult).then_inc(s_xa1, 1)
            dve.wait_ge(s_xa1, U)
            dve.tensor_tensor(zb[:], zb[:], beta2_row[:, L - 1:L, :].to_broadcast([P, T, D]), ALU.add).then_inc(s_xa, 1)
            dve.wait_ge(s_xa, U)
            dve.wait_ge(s_x0[w.par], 16 * (PL // 2))
            dve.tensor_tensor(stage[w.par][:], zb[:], stage[w.par][:], ALU.add).then_inc(s_fin, 1)
            bn_halves(2, stage[w.par], w.n - FIN0, s_fin, 1)
            mean_variance(2, w.n - FIN0)
            final_shift(w)

        @block.gpsimd
        def _(pool):
            def rstd(i, k):
                pool.wait_ge(s_mv[i], k + 1)
                if i == 2:
                    pool.wait_ge(s_norm3, k)
                pool.tensor_tensor(ve[i][:], mv[i][:, :, 1], eps_c[:], ALU.add).then_inc(s_ve[i], 1)
                pool.wait_ge(s_ve[i], k + 1)
                pool.tensor_tensor(rs[i][:], ve[i][:], mhalf_c[:], ALU.pow).then_inc(s_rs[i], 1)

            def across(r, l):
                return r[:, l:l + 1, :].to_broadcast([P, T, D])

            def skip_input(u, l):
                b = nrm[u.par][:]
                pool.wait_ge(s_nt, u.n + 1)
                pool.tensor_tensor(b, b, across(g1_row, l), ALU.mult).then_inc(s_hb1, 1)
                pool.wait_ge(s_hb1, u.n + 1)
                pool.tensor_tensor(b, b, across(shift1_row, l), ALU.add).then_inc(s_hb, 1)

            def new_x(w, l):
                pool.wait_ge(s_n2, w.n + 1)
                pool.tensor_tensor(zb[:], zb[:], across(g2_row, l), ALU.mult).then_inc(s_xa1, 1)
                pool.wait_ge(s_xa1, w.n + 1)
                pool.tensor_tensor(zb[:], zb[:], across(beta2_row, l), ALU.add).then_inc(s_xa, 1)

            def final_sum(w):
                pool.wait_ge(s_xa, w.n + 1)
                pool.wait_ge(s_x0[w.par], 16 * (w.half - FIN0 // 2 + 1))
                pool.tensor_tensor(stage[w.par][:], zb[:], stage[w.par][:], ALU.add).then_inc(s_fin, 1)

            def x_low(w):
                pool.wait_ge(s_xhi, w.n + 1)
                pool.tensor_tensor(x_lo[:], x_in[w.par][:], x_hi[:], ALU.subtract).then_inc(s_xlo, 1)

            pool.memset(ident[:], 1.0)
            pool.memset(neg_eye[:], -1.0)
            pool.memset(eps_c[:], EPS)
            pool.memset(mhalf_c[:], -0.5).then_inc(s_const, 1)
            pool.wait_ge(s_const, 1)
            pool.affine_select(out=ident[:], in_=ident[:], compare_op=ALU.is_equal, fill=0.0, base=0,
                               pattern=[[-1, P]], channel_multiplier=1).then_inc(s_ident, 1)
            for r in range(R):
                v = pool.affine_select(out=neg_eye[:, r, :], in_=neg_eye[:, r, :], compare_op=ALU.is_equal, fill=0.0,
                                       base=r * P, pattern=[[-1, N]], channel_multiplier=1)
            v.then_inc(s_const, 3)

            x_low(Unit(0, 0))
            rstd(0, 0)
            pool.wait_ge(s_row, 80)
            pool.tensor_tensor(shift1_row[:], shift1_row[:], b2_row, ALU.add).then_inc(s_shift, 1)
            pool.wait_ge(s_shift, 1)
            x_low(Unit(0, 1))

            def iteration(u, l, l_tail, mid, fin_tail, fin_, exp_, split):
                t = u.plus(-1)
                if l is not None:
                    skip_input(u, l)
                if l_tail is not None:
                    rstd(1, t.n)
                if l_tail is not None:
                    new_x(t, l_tail)
                if mid:
                    rstd(0, u.n + 1)
                if fin_:
                    rstd(2, u.n - 2 - FIN0)
                if fin_tail:
                    final_sum(t)
                if exp_:
                    x_low(u.plus(2))
                if split:
                    split_w2_low(pool, split)

            def key(u):
                return (layer(u), layer(u - 1), layer(u + 1) is not None and layer(u) is not None,
                        layer(u - 1) == L - 1, layer(u - 2) == L - 1, layer(u + 2) is not None,
                        w2_beside(u))

            keys = [(key(2 * j), key(2 * j + 1)) for j in range(PAIRS)]
            for a, b in runs(keys, CUTS):
                with over_pairs(pool, a, b) as j:
                    for c in range(2):
                        iteration(Unit(j, c), *keys[a][c])
            rstd(1, U - 1)
            rstd(2, U - 2 - FIN0)
            rstd(2, U - 1 - FIN0)


_INS = ['x', 'adj', 'L0_gnn_attn_w', 'L0_gnn_attn_b', 'L0_gnn_W1', 'L0_gnn_b1', 'L0_gnn_W2', 'L0_gnn_b2',
        'L0_gnn_g1', 'L0_gnn_beta1', 'L0_gnn_g2', 'L0_gnn_beta2']


def kernel(**inputs):
    import numpy as _np
    import concourse.bacc as _bacc
    from concourse import mybir as _mybir
    from concourse.bass_utils import run_bass_kernel_spmd as _run

    nc = _bacc.Bacc("TRN2", target_bir_lowering=False, num_devices=1)
    arrays, args = {}, []
    for name in _INS:
        a = _np.ascontiguousarray(inputs[name])
        arrays[f"in_{name}"] = a
        args.append(nc.dram_tensor(f"in_{name}", a.shape, _mybir.dt.from_np(a.dtype), kind="ExternalInput").ap())
    args.append(nc.dram_tensor("out_0", inputs['x'].shape, _mybir.dt.float32, kind="ExternalOutput").ap())
    gnn_kernel(nc, *args)
    r = _run(nc, [arrays], core_ids=[0])
    return r.results[0]["out_0"]
```
